# Optimizing a Trainium2 kernel written in Bass

```python
import numpy as np
import jax
import jax.numpy as jnp

def _softmax(x, axis=-1):
    return jax.nn.softmax(x, axis=axis)

def _gelu(x):
    return jax.nn.gelu(x, approximate=True)

def _silu(x):
    return jax.nn.silu(x)

def _sigmoid(x):
    return jax.nn.sigmoid(x)

def _layernorm(x, axis=-1, eps=1e-05):
    m = jnp.mean(x, axis=axis, keepdims=True)
    v = jnp.var(x, axis=axis, keepdims=True)
    return (x - m) / jnp.sqrt(v + eps)

def _scatter_add(tgt, idx, src, axis=0):
    return tgt.at[idx].add(src)

def _segment_sum(src, seg, n):
    return jax.ops.segment_sum(src, seg, n)
kernel_name = 'mk_rec_standalone_d1_rec_r8_a02c5e'

def setup_inputs(seed: int=0):
    np.random.seed(seed)
    _w = jnp.asarray

    def _rec_inputs():
        import jax
        import jax.numpy as jnp
        _rk = jax.random.key(seed)
        r_d_onehot = jax.random.bernoulli(jax.random.fold_in(_rk, 1), 0.1429, (1024, 7)).astype(jnp.float32)
        r_cat_b_ix = jax.random.randint(jax.random.fold_in(_rk, 2), (1024,), 9, 9999, jnp.int32)
        r_hvb_ix = jnp.stack([jax.random.randint(jax.random.fold_in(jax.random.fold_in(_rk, 3), 0), (1024,), 34, 49994, jnp.int32), jax.random.randint(jax.random.fold_in(jax.random.fold_in(_rk, 3), 1), (1024,), 31, 49999, jnp.int32), jax.random.randint(jax.random.fold_in(jax.random.fold_in(_rk, 3), 2), (1024,), 7, 6250, jnp.int32), jax.random.randint(jax.random.fold_in(jax.random.fold_in(_rk, 3), 3), (1024,), 5, 49901, jnp.int32), jax.random.randint(jax.random.fold_in(jax.random.fold_in(_rk, 3), 4), (1024,), 13, 49967, jnp.int32), jax.random.randint(jax.random.fold_in(jax.random.fold_in(_rk, 3), 5), (1024,), 7, 6249, jnp.int32), jax.random.randint(jax.random.fold_in(jax.random.fold_in(_rk, 3), 6), (1024,), 3, 49969, jnp.int32), jax.random.randint(jax.random.fold_in(jax.random.fold_in(_rk, 3), 7), (1024,), 11, 49979, jnp.int32)], axis=1)
        r_hvf_ix = jnp.stack([jax.random.randint(jax.random.fold_in(jax.random.fold_in(_rk, 4), 0), (1024,), 9, 49998, jnp.int32), jax.random.randint(jax.random.fold_in(jax.random.fold_in(_rk, 4), 1), (1024,), 41, 49957, jnp.int32), jax.random.randint(jax.random.fold_in(jax.random.fold_in(_rk, 4), 2), (1024,), 10, 49996, jnp.int32), jax.random.randint(jax.random.fold_in(jax.random.fold_in(_rk, 4), 3), (1024,), 18, 49972, jnp.int32), jax.random.randint(jax.random.fold_in(jax.random.fold_in(_rk, 4), 4), (1024,), 4, 49975, jnp.int32), jax.random.randint(jax.random.fold_in(jax.random.fold_in(_rk, 4), 5), (1024,), 1, 49949, jnp.int32), jax.random.randint(jax.random.fold_in(jax.random.fold_in(_rk, 4), 6), (1024,), 2, 49935, jnp.int32), jax.random.randint(jax.random.fold_in(jax.random.fold_in(_rk, 4), 7), (1024,), 32, 6249, jnp.int32)], axis=1)
        r_hvb_top = 0.00241105 + 0.999324 * jax.random.normal(jax.random.fold_in(_rk, 5), (1024, 256), jnp.float32)
        r_hvf_top = -0.00245836 + 0.999122 * jax.random.normal(jax.random.fold_in(_rk, 6), (1024, 256), jnp.float32)
        return (r_d_onehot, r_cat_b_ix, r_hvb_ix, r_hvf_ix, r_hvb_top, r_hvf_top)
    r_d_onehot, r_cat_b_ix, r_hvb_ix, r_hvf_ix, r_hvb_top, r_hvf_top = _rec_inputs()

    def _L0_rec_setup():
        import jax, jax.numpy as jnp
        import numpy as np
        B, NNZ = (256, 8)
        CAT_V, HVEC_V = (1250, 6250)
        SYN, SEM = (128, 256)
        HIDDEN, OUT = (1024, 1250)

        def _multi_hot(ix, vocab):
            rows = jnp.arange(ix.shape[0])[:, None]
            return jnp.zeros((ix.shape[0], vocab), dtype=jnp.float32).at[rows, ix].set(1.0)
        key = jax.random.key(seed)
        ks = jax.random.split(key, 12)
        d_onehot = jax.nn.one_hot(jax.random.randint(ks[0], (B,), 0, 7), 7, dtype=jnp.float32)
        cat_b_ix = jax.random.randint(ks[1], (B,), 0, CAT_V)
        hvb_ix = jax.random.randint(ks[2], (B, NNZ), 0, HVEC_V)
        hvf_ix = jax.random.randint(ks[3], (B, NNZ), 0, HVEC_V)
        hvb_top = jax.random.normal(ks[4], (B, SEM), dtype=jnp.float32)
        hvf_top = jax.random.normal(ks[5], (B, SEM), dtype=jnp.float32)
        cat_embeds = jax.random.normal(ks[6], (CAT_V, SYN), dtype=jnp.float32) * 0.02
        hvec_embeds = jax.random.normal(ks[7], (HVEC_V, SEM), dtype=jnp.float32) * 0.02
        in_dim = 7 + SYN + 2 * SEM
        W1 = jax.random.normal(ks[8], (HIDDEN, in_dim), dtype=jnp.float32) / np.sqrt(in_dim)
        b1 = jnp.zeros((HIDDEN,), dtype=jnp.float32)
        W2 = jax.random.normal(ks[9], (OUT, HIDDEN), dtype=jnp.float32) / np.sqrt(HIDDEN)
        b2 = jnp.zeros((OUT,), dtype=jnp.float32)
        return {'d_onehot': d_onehot, 'cat_b_ix': cat_b_ix, 'hvb_ix': hvb_ix, 'hvf_ix': hvf_ix, 'hvb_top': hvb_top, 'hvf_top': hvf_top, 'cat_embeds': cat_embeds, 'hvec_embeds': hvec_embeds, 'W1': W1, 'b1': b1, 'W2': W2, 'b2': b2}
    _L0_rec_all = _L0_rec_setup()
    _L0_rec_in = {k: v for k, v in _L0_rec_all.items() if k in ('cat_embeds', 'hvec_embeds', 'W1', 'b1', 'W2', 'b2')}
    del _L0_rec_all
    return {'r_d_onehot': r_d_onehot, 'r_cat_b_ix': r_cat_b_ix, 'r_hvb_ix': r_hvb_ix, 'r_hvf_ix': r_hvf_ix, 'r_hvb_top': r_hvb_top, 'r_hvf_top': r_hvf_top, 'L0_rec_cat_embeds': _L0_rec_in['cat_embeds'], 'L0_rec_hvec_embeds': _L0_rec_in['hvec_embeds'], 'L0_rec_W1': _L0_rec_in['W1'], 'L0_rec_b1': _L0_rec_in['b1'], 'L0_rec_W2': _L0_rec_in['W2'], 'L0_rec_b2': _L0_rec_in['b2']}

def reference(r_d_onehot, r_cat_b_ix, r_hvb_ix, r_hvf_ix, r_hvb_top, r_hvf_top, L0_rec_cat_embeds, L0_rec_hvec_embeds, L0_rec_W1, L0_rec_b1, L0_rec_W2, L0_rec_b2):
    import jax
    import jax.numpy as jnp

    def _L0_rec_ref(d_onehot, cat_b_ix, hvb_ix, hvf_ix, hvb_top, hvf_top, cat_embeds, hvec_embeds, W1, b1, W2, b2):
        import jax, jax.numpy as jnp
        import numpy as np
        B, NNZ = (256, 8)
        CAT_V, HVEC_V = (1250, 6250)
        SYN, SEM = (128, 256)
        HIDDEN, OUT = (1024, 1250)

        def _multi_hot(ix, vocab):
            rows = jnp.arange(ix.shape[0])[:, None]
            return jnp.zeros((ix.shape[0], vocab), dtype=jnp.float32).at[rows, ix].set(1.0)
        cat_b_embed = cat_embeds[cat_b_ix]
        hvb_mat = _multi_hot(hvb_ix, hvec_embeds.shape[0])
        hvf_mat = _multi_hot(hvf_ix, hvec_embeds.shape[0])
        hvb_embed = hvb_mat @ hvec_embeds + hvb_top
        hvf_embed = hvf_mat @ hvec_embeds + hvf_top
        x = jnp.concatenate([cat_b_embed, hvb_embed, hvf_embed, d_onehot], axis=1)
        x = jax.nn.relu(x @ W1.T + b1)
        x = x @ W2.T + b2
        return jax.nn.log_softmax(x, axis=1)
    y = _L0_rec_ref(r_d_onehot, r_cat_b_ix, r_hvb_ix, r_hvf_ix, r_hvb_top, r_hvf_top, L0_rec_cat_embeds, L0_rec_hvec_embeds, L0_rec_W1, L0_rec_b1, L0_rec_W2, L0_rec_b2)
    return y

_drawn_inputs = setup_inputs


def setup_inputs(seed=0):
    import zlib

    import numpy as np

    out = dict(_drawn_inputs(seed))
    spreads = {'L0_rec_b1': (0.0, 0.8), 'L0_rec_b2': (0.0, 0.581)}
    factors = {'r_d_onehot': 8.0, 'L0_rec_cat_embeds': 64.0, 'L0_rec_hvec_embeds': 23.5}
    for name, (base, spread) in spreads.items():
        noise = np.random.default_rng([zlib.crc32(name.encode()), seed]).standard_normal(out[name].shape)
        drawn = base * np.exp(spread * noise) if base else spread * noise
        out[name] = jnp.asarray(drawn.astype(out[name].dtype))
    for name, factor in factors.items():
        out[name] = (out[name] * factor).astype(out[name].dtype)
    return out
```

```python
import concourse.bass as bass
from concourse import mybir
from contextlib import ExitStack

F32, F32R, I32, BF16 = mybir.dt.float32, mybir.dt.float32r, mybir.dt.int32, mybir.dt.bfloat16
ALU = mybir.AluOpType
ACT = mybir.ActivationFunctionType
AX = mybir.AxisListType

P = 128
BATCH, NNZ = 1024, 8
SYN, SEM = 128, 256
CAT_V, HVEC_V = 1250, 6250
HIDDEN, OUT = 1024, 1250
NDIR = 7
TILES = BATCH // P
NIX = 2 * NNZ + 1
XK = (SYN + 2 * SEM) // P
HK = HIDDEN // P
NC1 = 512
NCH = 3
CW = 418
OUTP = NCH * CW
TAIL = NDIR + 1
LO_ROW = 64
TAILK = LO_ROW + TAIL
MARK = 8192.0
PADB = -3.0e38
SLOTS = NNZ + 1


def build(nc, ix_d, oneh_d, hvb_top, hvf_top, cat_tab, hvec_tab, w1t, w1tail_d, w2t, b2_d, out):
    with ExitStack() as ctx:
        def sb(name, shape, dt=F32):
            return ctx.enter_context(nc.sbuf_tensor(name, shape, dt))

        def pb(name, shape):
            return ctx.enter_context(nc.psum_tensor(name, shape, F32))

        def sem(name):
            return ctx.enter_context(nc.semaphore(name))

        w1_hi = sb("w1_hi", [P, XK, HIDDEN], F32R)
        w1_lo = sb("w1_lo", [P, XK, HIDDEN], F32R)
        w1_tail = sb("w1_tail", [TAILK, HIDDEN], F32R)
        w2_hi = sb("w2_hi", [P, HK, OUTP], F32R)
        w2_lo = sb("w2_lo", [P, HK, OUTP], F32R)
        b2_all = sb("b2_all", [P, OUTP])
        identity = sb("identity", [P, P])
        rows = sb("rows", [P, 3, OUTP])
        ix_raw = sb("ix_raw", [P, TILES, NIX], I32)
        ix_f = sb("ix_f", [P, TILES, NIX])
        ix_neg = sb("ix_neg", [P, TILES, NIX])
        ix_key = sb("ix_key", [P, TILES, NIX])
        ix_sort = sb("ix_sort", [P, TILES, 2 * NNZ])
        ix_bad = sb("ix_bad", [P, TILES, 2 * NNZ])
        ix_dup = sb("ix_dup", [P, TILES, 2, NNZ])
        ix_all = sb("ix_all", [P, TILES, NIX], I32)
        ix_now = sb("ix_now", [P, 2, NIX], I32)
        w1_tail_raw = sb("w1_tail_raw", [TAILK, HIDDEN])
        got = [sb("got_b", [P, SLOTS * SEM]), sb("got_f", [P, SLOTS * SEM])]
        got_cat = sb("got_cat", [P, SYN])
        x_sum = sb("x_sum", [P, 2, XK * P])
        x_hi = sb("x_hi", [P, XK * P], F32R)
        x_lo = sb("x_lo", [P, XK * P], F32R)
        oneh = sb("oneh", [TAILK, BATCH])
        x_tail = sb("x_tail", [TAILK, 2, P], F32R)
        h_act = sb("h_act", [P, HIDDEN])
        h_hi = sb("h_hi", [P, 2, HIDDEN], F32R)
        h_lo = sb("h_lo", [P, 2, HIDDEN], F32R)
        exps = sb("exps", [P, OUTP], BF16)
        maxes = sb("maxes", [P, 2, NCH])
        neg_max = sb("neg_max", [P, 2])
        exp_sum = sb("exp_sum", [P, 2])
        log_sum = sb("log_sum", [P, 2])
        turned = pb("turned", [P, 2 * NC1])
        hid = pb("hid", [P, HIDDEN])
        logit = pb("logit", [P, NCH, NC1])

        ix_loaded, ix_step = sem("ix_loaded"), sem("ix_step")
        ix_staged = [sem("ix_staged0"), sem("ix_staged1")]
        cat_free = [sem("cat_free0"), sem("cat_free1")]
        oneh_loaded, oneh_clear = sem("oneh_loaded"), sem("oneh_clear")
        row_loaded = [sem(f"row_loaded{i}") for i in range(3)]
        b2_loaded = sem("b2_loaded")
        pads_set, ident_zero, ident_done = sem("pads_set"), sem("ident_zero"), sem("ident_done")
        w_hi_done, w_lo_done = sem("w_hi_done"), sem("w_lo_done")
        tail_w_loaded, tail_w_done = sem("tail_w_loaded"), sem("tail_w_done")
        zeroed = [[sem(f"zeroed_{g}{u}") for u in range(2)] for g in "bf"]
        top_loaded = [sem("top_b_loaded"), sem("top_f_loaded")]
        gathered = [sem("gathered_b"), sem("gathered_f")]
        cat_gathered, cat_copied = sem("cat_gathered"), sem("cat_copied")
        summed = [sem("summed_b"), sem("summed_f")]
        x_turned, x_hi_done, x_lo_done = sem("x_turned"), sem("x_hi_done"), sem("x_lo_done")
        tail_hi_done, tail_lo_done = sem("tail_hi_done"), sem("tail_lo_done")
        hid_done, act_done = sem("hid_done"), sem("act_done")
        h_turned, h_hi_done, h_lo_done = sem("h_turned"), sem("h_hi_done"), sem("h_lo_done")
        logit_done = [sem(f"logit_done{c}") for c in range(NCH)]
        bank_free = [sem(f"bank_free{c}") for c in range(NCH)]
        row_free = [sem("row_free0"), sem("row_free1")]
        max_done, exp_done, log_done = sem("max_done"), sem("exp_done"), sem("log_done")
        result_done = sem("result_done")
        stored = [sem("stored0"), sem("stored1")]

        pieces = [(w1t[k * P:(k + 1) * P, :], HIDDEN, w1_hi[:, k, :], w1_lo[:, k, :]) for k in range(XK)]
        pieces += [(w2t[k * P:(k + 1) * P, :], OUT, w2_hi[:, k, 0:OUT], w2_lo[:, k, 0:OUT]) for k in range(HK)]

        block = ctx.enter_context(nc.Block())

        @block.sync
        def _(sp):
            sp.dma_start(ix_raw[:], ix_d).then_inc(ix_loaded, 16)
            for g, top in enumerate((hvb_top, hvf_top)):
                sp.dma_start(got[g][:, NNZ * SEM:], top[0:P, :]).then_inc(top_loaded[g], 16)
            sp.wait_ge(oneh_clear, 2)
            for at in (0, 32, LO_ROW):
                sp.dma_start(oneh[at:at + TAIL, :], oneh_d).then_inc(oneh_loaded, 16)
                sp.dma_start(w1_tail_raw[at:at + TAIL, :], w1tail_d).then_inc(tail_w_loaded, 16)
            for n, (src, width, _, _) in enumerate(pieces):
                if n >= 3:
                    sp.wait_ge(w_lo_done, n - 2)
                sp.dma_start(rows[:, n % 3, 0:width], src).then_inc(row_loaded[n % 3], 16)
            sp.dma_start(b2_all[:, 0:OUT], b2_d.to_broadcast([P, OUT])).then_inc(b2_loaded, 16)

            def load_tops(t):
                for g, top in enumerate((hvb_top, hvf_top)):
                    sp.wait_ge(summed[g], t)
                    sp.dma_start(got[g][:, NNZ * SEM:], top[bass.ds(t * P, P), :]).then_inc(top_loaded[g], 16)

            def store(t, u):
                sp.wait_ge(result_done, t + 1)
                sp.dma_start(out[bass.ds(t * P, P), :], rows[:, u, 0:OUT]).then_inc(stored[u], 16)

            def free_row(i, u):
                sp.wait_ge(stored[u], 16 * i)
                sp.sem_inc(row_free[u], 1)

            load_tops(1)
            for t in range(2):
                load_tops(t + 2)
                store(t, t)
            with sp.Fori(1, TILES // 2 - 1) as i:
                for u in range(2):
                    free_row(i, u)
                    load_tops(2 * i + u + 2)
                    store(2 * i + u, u)
            for u in range(2):
                free_row(TILES // 2 - 1, u)
                store(TILES - 2 + u, u)
            for u in range(2):
                sp.wait_ge(stored[u], 16 * (TILES // 2))

        @block.gpsimd
        def _(pool):
            pool.memset(oneh[:], 0.0).then_inc(oneh_clear, 1)
            pool.memset(w1_tail_raw[:], 0.0).then_inc(oneh_clear, 1)
            for g in range(2):
                pool.memset(got[g][:, 0:NNZ * SEM], 0.0).then_inc(zeroed[g][0], 1)
            pool.memset(identity[:], 0.0).then_inc(ident_zero, 1)
            pool.wait_ge(ident_zero, 1)
            pool.affine_select(out=identity[:], in_=identity[:], compare_op=ALU.not_equal, fill=1.0, base=0,
                               pattern=[[-1, P]], channel_multiplier=1).then_inc(ident_done, 1)

            last_hvec, last_cat = pool.to_reg(HVEC_V - 1), pool.to_reg(CAT_V - 1)

            def gather(n, u):
                for g in range(2):
                    pool.wait_ge(ix_loaded, 16)
                    pool.wait_ge(ix_staged[u], n)
                    pool.wait_ge(zeroed[g][u], n)
                    for j in range(NNZ):
                        at = g * NNZ + j
                        pool.indirect_dma_start(
                            out=got[g][:, j * SEM:(j + 1) * SEM], out_offset=None, in_=hvec_tab,
                            in_offset=bass.IndirectOffsetOnAxis(ap=ix_now[:, u, at:at + 1], axis=0),
                            bounds_check=last_hvec, oob_is_err=False).then_inc(gathered[g], 16)
                pool.wait_ge(ix_loaded, 16)
                pool.wait_ge(cat_free[u], n)
                pool.indirect_dma_start(
                    out=got_cat[:], out_offset=None, in_=cat_tab,
                    in_offset=bass.IndirectOffsetOnAxis(ap=ix_now[:, u, NIX - 1:NIX], axis=0),
                    bounds_check=last_cat, oob_is_err=False).then_inc(cat_gathered, 16)

            with pool.Fori(1, TILES // 2 + 1) as n:
                for u in range(2):
                    gather(n, u)

        @block.scalar
        def _(act):
            act.wait_ge(oneh_loaded, 48)

            def zero(g, t, u):
                act.wait_ge(summed[g], t)
                act.memzero(got[g][:, 0:NNZ * SEM]).then_inc(zeroed[g][u], 1)

            def tail_hi(t, u):
                act.copy(x_tail[:, u, :], oneh[:, bass.ds(t * P, P)]).then_inc(tail_hi_done, 1)

            def x_high(t):
                act.wait_ge(x_turned, t + 1)
                act.copy(x_hi[:], turned[:, 0:XK * P]).then_inc(x_hi_done, 1)

            def relu(t):
                act.wait_ge(hid_done, t + 1)
                act.activation(h_act[:], hid[:], ACT.Relu).then_inc(act_done, 1)

            def h_high(t, u):
                for half in range(2):
                    act.wait_ge(h_turned, 2 * t + half + 1)
                    act.copy(h_hi[:, u, half * NC1:(half + 1) * NC1],
                             turned[:, half * NC1:(half + 1) * NC1]).then_inc(h_hi_done, 1)

            def softmax_sum(t, u):
                act.wait_ge(max_done, t + 1)
                act.activation(exps[:], rows[:, u, :], ACT.Exp, bias=neg_max[:, u:u + 1],
                               accum_out=exp_sum[:, u:u + 1]).then_inc(exp_done, 1)
                act.wait_ge(exp_done, t + 1)
                act.activation(log_sum[:, u:u + 1], exp_sum[:, u:u + 1], ACT.Ln).then_inc(log_done, 1)

            def split_high(n):
                act.wait_ge(row_loaded[n % 3], 16 * (n // 3 + 1))
                act.copy(pieces[n][2], rows[:, n % 3, 0:pieces[n][1]]).then_inc(w_hi_done, 1)

            tail_hi(0, 0)
            act.wait_ge(tail_w_loaded, 48)
            act.copy(w1_tail[:], w1_tail_raw[:]).then_inc(tail_w_done, 1)
            for n in range(XK + 2):
                split_high(n)
            zero(0, 1, 1)
            for n in range(XK + 2, XK + 5):
                split_high(n)
            x_high(0)
            zero(1, 1, 1)
            relu(0)
            for n in range(XK + 5, XK + HK):
                split_high(n)
            h_high(0, 0)
            zero(0, 2, 0)

            def step(t, u, more):
                if more:
                    zero(1, t + 2, u)
                x_high(t + 1)
                tail_hi(t + 1, 1 - u)
                relu(t + 1)
                if more:
                    zero(0, t + 3, 1 - u)
                h_high(t + 1, 1 - u)
                softmax_sum(t, u)

            with act.Fori(0, TILES // 2 - 1) as i:
                for u in range(2):
                    step(2 * i + u, u, True)
            step(TILES - 2, 0, False)
            softmax_sum(TILES - 1, 1)

        @block.vector
        def _(dve):
            steps = [0]

            def link(ins):
                steps[0] += 1
                ins.then_inc(ix_step, 1)
                dve.wait_ge(ix_step, steps[0])

            HV = 2 * NNZ
            for free in (cat_free[0], *bank_free, *row_free):
                dve.sem_inc(free, 1)
            dve.memset(b2_all[:, OUT:], PADB).then_inc(pads_set, 1)
            dve.memset(w2_hi[:, :, OUT:].bitcast(F32), 0.0).then_inc(pads_set, 1)
            dve.memset(w2_lo[:, :, OUT:].bitcast(F32), 0.0).then_inc(pads_set, 1)
            dve.wait_ge(ix_loaded, 16)
            link(dve.tensor_copy(ix_f[:], ix_raw[:]))
            dve.tensor_scalar(ix_neg[:, :, 0:HV], ix_f[:, :, 0:HV], 0.0, float(HVEC_V), ALU.is_lt, ALU.mult)
            link(dve.tensor_scalar(ix_neg[:, :, HV:], ix_f[:, :, HV:], 0.0, float(CAT_V), ALU.is_lt, ALU.mult))
            link(dve.tensor_tensor(ix_f[:], ix_f[:], ix_neg[:], ALU.add))
            link(dve.tensor_scalar(ix_key[:, :, HV:], ix_f[:, :, HV:], 0.0, float(CAT_V - 1), ALU.max, ALU.min))
            link(dve.tensor_copy(ix_all[:, :, HV:], ix_key[:, :, HV:]))
            link(dve.tensor_scalar(ix_neg[:, :, 0:HV], ix_f[:, :, 0:HV], 1.0, None, ALU.add))
            link(dve.scalar_tensor_tensor(out=ix_key[:, :, 0:HV], in0=ix_f[:, :, 0:HV], scalar=float(HVEC_V - 1),
                                          in1=ix_neg[:, :, 0:HV], op0=ALU.is_le, op1=ALU.mult))
            for t in range(TILES):
                for g in range(2):
                    last = dve.max(ix_sort[:, t, g * NNZ:(g + 1) * NNZ], ix_key[:, t, g * NNZ:(g + 1) * NNZ])
            link(last)
            link(dve.tensor_scalar(ix_bad[:], ix_sort[:], 0.0, MARK, ALU.is_le, ALU.mult))
            sorted4 = ix_sort[:].rearrange("p t (g j) -> p (t g) j", g=2)
            bad4 = ix_bad[:].rearrange("p t (g j) -> p (t g) j", g=2)
            dup4 = ix_dup[:].rearrange("p t g j -> p (t g) j")
            link(dve.tensor_tensor(dup4[:, :, 1:], sorted4[:, :, 1:], sorted4[:, :, :NNZ - 1], ALU.is_equal))
            link(dve.scalar_tensor_tensor(out=bad4[:, :, 1:], in0=dup4[:, :, 1:], scalar=MARK,
                                          in1=bad4[:, :, 1:], op0=ALU.mult, op1=ALU.add))
            link(dve.tensor_scalar(ix_sort[:], ix_sort[:], 0.0, -1.0, ALU.max, ALU.add))
            link(dve.tensor_tensor(ix_all[:, :, 0:HV], ix_sort[:], ix_bad[:], ALU.add))

            def stage(t, u):
                dve.tensor_copy(ix_now[:, u, :], ix_all[:, bass.ds(t, 1), :]
                                .rearrange("p a n -> p (a n)")).then_inc(ix_staged[u], 1)

            def sum_rows(g, t, u):
                dve.wait_ge(gathered[g], 16 * NNZ * (t + 1))
                dve.wait_ge(top_loaded[g], 16 * (t + 1))
                at = SYN + g * SEM
                dve.tensor_reduce(x_sum[:, u, at:at + SEM], got[g][:].rearrange("p (s d) -> p d s", s=SLOTS),
                                  AX.X, ALU.add).then_inc(summed[g], 1)

            def take_cat(t, u):
                dve.wait_ge(cat_gathered, 16 * (t + 1))
                dve.tensor_copy(x_sum[:, u, 0:SYN], got_cat[:]).then_inc(cat_copied, 1)
                dve.wait_ge(cat_copied, t + 1)
                dve.sem_inc(cat_free[1 - u], 1)

            def x_low(t):
                dve.wait_ge(x_hi_done, t + 1)
                dve.tensor_tensor(x_lo[:], turned[:, 0:XK * P], x_hi[:].bitcast(F32),
                                  ALU.subtract).then_inc(x_lo_done, 1)

            def tail_low(t, u):
                dve.wait_ge(tail_hi_done, t + 1)
                dve.tensor_tensor(x_tail[LO_ROW:TAILK, u, :], oneh[LO_ROW:TAILK, bass.ds(t * P, P)],
                                  x_tail[LO_ROW:TAILK, u, :].bitcast(F32), ALU.subtract).then_inc(tail_lo_done, 1)

            def h_low(t, u):
                for half in range(2):
                    cols = slice(half * NC1, (half + 1) * NC1)
                    dve.wait_ge(h_hi_done, 2 * t + half + 1)
                    dve.tensor_tensor(h_lo[:, u, cols], turned[:, cols], h_hi[:, u, cols].bitcast(F32),
                                      ALU.subtract).then_inc(h_lo_done, 1)

            def take_logits(c, now, u):
                dve.wait_ge(logit_done[c], now)
                cols = slice(c * CW, (c + 1) * CW)
                dve.tensor_tensor_reduce(rows[:, u, cols], logit[:, c, 0:CW], b2_all[:, cols], 1.0, -3.4e38,
                                         ALU.add, ALU.max, maxes[:, u, c:c + 1]).then_inc(bank_free[c], 1)

            def row_max(t, u):
                for c in range(NCH):
                    dve.wait_ge(bank_free[c], t + 2)
                dve.tensor_reduce(neg_max[:, u:u + 1], maxes[:, u, :], AX.X, ALU.max,
                                  negate=True).then_inc(max_done, 1)

            def result(t, u):
                dve.wait_ge(log_done, t + 1)
                dve.tensor_scalar(rows[:, u, 0:OUT], rows[:, u, 0:OUT], neg_max[:, u:u + 1], log_sum[:, u:u + 1],
                                  ALU.add, ALU.subtract).then_inc(result_done, 1)

            def split_low(n):
                dve.wait_ge(w_hi_done, n + 1)
                _, width, high, low = pieces[n]
                dve.tensor_tensor(low, rows[:, n % 3, 0:width], high.bitcast(F32), ALU.subtract)\
                   .then_inc(w_lo_done, 1)

            stage(0, 0)
            stage(1, 1)
            dve.wait_ge(pads_set, 3)
            for n in range(XK):
                split_low(n)
            tail_low(0, 0)
            dve.wait_ge(tail_w_done, 1)
            dve.tensor_tensor(w1_tail[32:32 + TAIL, :], w1_tail_raw[32:32 + TAIL, :],
                              w1_tail[32:32 + TAIL, :].bitcast(F32), ALU.subtract).then_inc(tail_w_done, 1)
            sum_rows(0, 0, 0)
            for n in range(XK, XK + 5):
                split_low(n)
            sum_rows(1, 0, 0)
            take_cat(0, 0)
            x_low(0)
            for n in range(XK + 5, XK + HK):
                split_low(n)
            sum_rows(0, 1, 1)
            h_low(0, 0)

            def step(t, u, i, more):
                now = t + 1
                dve.wait_ge(row_free[u], i + 1)
                dve.wait_ge(x_turned, now)
                sum_rows(1, t + 1, 1 - u)
                take_cat(t + 1, 1 - u)
                dve.wait_ge(b2_loaded, 16)
                take_logits(0, now, u)
                x_low(t + 1)
                tail_low(t + 1, 1 - u)
                dve.wait_ge(b2_loaded, 16)
                take_logits(1, now, u)
                if more:
                    stage(t + 2, u)
                    sum_rows(0, t + 2, u)
                h_low(t + 1, 1 - u)
                dve.wait_ge(b2_loaded, 16)
                take_logits(2, now, u)
                row_max(t, u)
                result(t, u)

            with dve.Fori(0, TILES // 2 - 1) as i:
                for u in range(2):
                    step(2 * i + u, u, i, True)
            step(TILES - 2, 0, TILES // 2 - 1, False)
            last = TILES - 1
            dve.wait_ge(row_free[1], TILES // 2)
            for c in range(NCH):
                take_logits(c, last + 1, 1)
            row_max(last, 1)
            result(last, 1)

        @block.tensor
        def _(pe):
            def turn_x(t, u):
                for s in (summed[0], summed[1], cat_copied):
                    pe.wait_ge(s, t + 1)
                for k in range(XK):
                    last = pe.transpose(turned[:, k * P:(k + 1) * P], x_sum[:, u, k * P:(k + 1) * P], identity[:])
                last.then_inc(x_turned, 1)

            def first_layer(t, u):
                pe.wait_ge(x_hi_done, t + 1)
                pe.wait_ge(x_lo_done, t + 1)
                pe.wait_ge(tail_lo_done, t + 1)
                for n in range(HIDDEN // NC1):
                    cols = slice(n * NC1, (n + 1) * NC1)
                    pe.matmul(hid[:, cols], x_tail[:, u, :], w1_tail[:, cols], start=True, stop=False)
                    for k in range(XK):
                        xs = slice(k * P, (k + 1) * P)
                        pe.matmul(hid[:, cols], x_hi[:, xs], w1_hi[:, k, cols], start=False, stop=False)
                        pe.matmul(hid[:, cols], x_hi[:, xs], w1_lo[:, k, cols], start=False, stop=False)
                        last = pe.matmul(hid[:, cols], x_lo[:, xs], w1_hi[:, k, cols],
                                         start=False, stop=k == XK - 1)
                last.then_inc(hid_done, 1)

            def turn_h(t):
                pe.wait_ge(act_done, t + 1)
                for k in range(HK):
                    ins = pe.transpose(turned[:, k * P:(k + 1) * P], h_act[:, k * P:(k + 1) * P], identity[:])
                    if k % (HK // 2) == HK // 2 - 1:
                        ins.then_inc(h_turned, 1)

            def second_layer(c, t, u, k0=0, k1=HK):
                if k0 == 0:
                    pe.wait_ge(bank_free[c], t + 1)
                cols = slice(c * CW, (c + 1) * CW)
                for k in range(k0, k1):
                    if c == 0 and k % (HK // 2) == 0:
                        pe.wait_ge(h_hi_done, 2 * t + 1 + k // (HK // 2))
                        pe.wait_ge(h_lo_done, 2 * t + 1 + k // (HK // 2))
                    ks = slice(k * P, (k + 1) * P)
                    pe.matmul(logit[:, c, 0:CW], h_hi[:, u, ks], w2_hi[:, k, cols], start=k == 0, stop=False)
                    pe.matmul(logit[:, c, 0:CW], h_hi[:, u, ks], w2_lo[:, k, cols], start=False, stop=False)
                    last = pe.matmul(logit[:, c, 0:CW], h_lo[:, u, ks], w2_hi[:, k, cols],
                                     start=False, stop=k == HK - 1)
                if k1 == HK:
                    last.then_inc(logit_done[c], 1)

            pe.wait_ge(ident_done, 1)
            turn_x(0, 0)
            pe.wait_ge(w_lo_done, XK)
            pe.wait_ge(tail_w_done, 2)
            first_layer(0, 0)
            turn_h(0)
            pe.wait_ge(w_lo_done, XK + HK)
            pe.wait_ge(pads_set, 3)

            def step(t, u):
                second_layer(0, t, u)
                turn_x(t + 1, 1 - u)
                second_layer(1, t, u)
                first_layer(t + 1, 1 - u)
                second_layer(2, t, u, 0, HK // 2)
                turn_h(t + 1)
                second_layer(2, t, u, HK // 2, HK)

            with pe.Fori(0, TILES // 2 - 1) as i:
                for u in range(2):
                    step(2 * i + u, u)
            step(TILES - 2, 0)
            for c in range(NCH):
                second_layer(c, TILES - 1, 1)


def kernel(r_d_onehot, r_cat_b_ix, r_hvb_ix, r_hvf_ix, r_hvb_top, r_hvf_top, L0_rec_cat_embeds,
           L0_rec_hvec_embeds, L0_rec_W1, L0_rec_b1, L0_rec_W2, L0_rec_b2):
    import numpy as np
    import concourse.bacc as bacc
    from concourse.bass_utils import run_bass_kernel_spmd as run

    ix = np.concatenate([np.asarray(r_hvb_ix), np.asarray(r_hvf_ix), np.asarray(r_cat_b_ix)[:, None]], axis=1)
    ix = ix.reshape(TILES, P, NIX).transpose(1, 0, 2)
    w1t = np.asarray(L0_rec_W1).T
    embedded = SYN + 2 * SEM
    ins = {
        "ix": ix,
        "oneh": np.concatenate([np.asarray(r_d_onehot).T, np.ones((1, BATCH), np.float32)], axis=0),
        "hvb_top": r_hvb_top,
        "hvf_top": r_hvf_top,
        "cat_tab": L0_rec_cat_embeds,
        "hvec_tab": L0_rec_hvec_embeds,
        "w1t": w1t[:embedded],
        "w1tail": np.concatenate([w1t[embedded:], np.asarray(L0_rec_b1)[None, :]], axis=0),
        "w2t": np.asarray(L0_rec_W2).T,
        "b2": np.asarray(L0_rec_b2)[None, :],
    }
    nc = bacc.Bacc("TRN2", target_bir_lowering=False, num_devices=1)
    arrays, args = {}, []
    for name, a in ins.items():
        a = np.ascontiguousarray(a)
        arrays[name + "_dram"] = a
        args.append(nc.dram_tensor(name + "_dram", a.shape, mybir.dt.from_np(a.dtype), kind="ExternalInput").ap())
    args.append(nc.dram_tensor("out_dram", (BATCH, OUT), F32, kind="ExternalOutput").ap())
    build(nc, *args)
    return run(nc, [arrays], core_ids=[0]).results[0]["out_dram"]
```

```python
import concourse.bass as bass
from concourse import mybir
from contextlib import ExitStack

F32, F32R, I32, BF16 = mybir.dt.float32, mybir.dt.float32r, mybir.dt.int32, mybir.dt.bfloat16
ALU = mybir.AluOpType
ACT = mybir.ActivationFunctionType
AX = mybir.AxisListType

P = 128
BATCH, NNZ = 1024, 8
SYN, SEM = 128, 256
CAT_V, HVEC_V = 1250, 6250
HIDDEN, OUT = 1024, 1250
NDIR = 7
TILES = BATCH // P
NIX = 2 * NNZ + 1
XK = (SYN + 2 * SEM) // P
HK = HIDDEN // P
NC1 = 512
NCH = 3
CW = 418
OUTP = NCH * CW
TAIL = NDIR + 1
LO_ROW = 64
TAILK = LO_ROW + TAIL
MARK = 8192.0
PADB = -3.0e38
XA = SYN + SEM
SLOTS = NNZ + 1


def build(nc, ix_d, oneh_d, hvb_top, hvf_top, cat_tab, hvec_tab, w1t, w1tail_d, w2t, b2_d, out):
    with ExitStack() as ctx:
        def sb(name, shape, dt=F32):
            return ctx.enter_context(nc.sbuf_tensor(name, shape, dt))

        def pb(name, shape):
            return ctx.enter_context(nc.psum_tensor(name, shape, F32))

        def sem(name):
            return ctx.enter_context(nc.semaphore(name))

        w1_hi = sb("w1_hi", [P, XK, HIDDEN], F32R)
        w1_lo = sb("w1_lo", [P, XK, HIDDEN], F32R)
        w1_tail = sb("w1_tail", [TAILK, HIDDEN], F32R)
        w2_hi = sb("w2_hi", [P, HK, OUTP], F32R)
        w2_lo = sb("w2_lo", [P, HK, OUTP], F32R)
        b2_all = sb("b2_all", [P, OUTP])
        identity = sb("identity", [P, P])
        rows = sb("rows", [P, 3, OUTP])
        ix_raw = sb("ix_raw", [P, TILES, NIX], I32)
        ix_f = sb("ix_f", [P, TILES, NIX])
        ix_neg = sb("ix_neg", [P, TILES, NIX])
        ix_key = sb("ix_key", [P, TILES, NIX])
        ix_sort = sb("ix_sort", [P, TILES, 2 * NNZ])
        ix_bad = sb("ix_bad", [P, TILES, 2 * NNZ])
        ix_dup = sb("ix_dup", [P, TILES, 2, NNZ])
        ix_all = sb("ix_all", [P, TILES, NIX], I32)
        ix_now = sb("ix_now", [P, 2, NIX], I32)
        w1_tail_raw = sb("w1_tail_raw", [TAILK, HIDDEN])
        got = [sb("got_b", [P, SLOTS * SEM]), sb("got_f", [P, SLOTS * SEM])]
        got_cat = sb("got_cat", [P, SYN])
        x_sum = sb("x_sum", [P, 2, XK * P])
        x_hi = sb("x_hi", [P, XK * P], F32R)
        x_lo = sb("x_lo", [P, XK * P], F32R)
        oneh = sb("oneh", [TAILK, BATCH])
        x_tail = sb("x_tail", [TAILK, 2, P], F32R)
        h_act = sb("h_act", [P, HIDDEN])
        h_hi = sb("h_hi", [P, 2, HIDDEN], F32R)
        h_lo = sb("h_lo", [P, 2, HIDDEN], F32R)
        exps = sb("exps", [P, OUTP], BF16)
        maxes = sb("maxes", [P, 2, NCH])
        neg_max = sb("neg_max", [P, 2])
        exp_sum = sb("exp_sum", [P, 2])
        log_sum = sb("log_sum", [P, 2])
        turned = pb("turned", [P, 2 * NC1])
        hid = pb("hid", [P, HIDDEN])
        logit = pb("logit", [P, NCH, NC1])

        ix_loaded, ix_step = sem("ix_loaded"), sem("ix_step")
        ix_staged = [sem("ix_staged0"), sem("ix_staged1")]
        cat_free = [sem("cat_free0"), sem("cat_free1")]
        oneh_loaded, tails_clear = sem("oneh_loaded"), sem("tails_clear")
        row_loaded = [sem(f"row_loaded{i}") for i in range(3)]
        b2_loaded = sem("b2_loaded")
        pads_set, ident_zero, ident_done = sem("pads_set"), sem("ident_zero"), sem("ident_done")
        w_hi_done, w_lo_done = sem("w_hi_done"), sem("w_lo_done")
        tail_w_loaded, tail_w_done = sem("tail_w_loaded"), sem("tail_w_done")
        zeroed = [[sem(f"zeroed_{g}{u}") for u in range(2)] for g in "bf"]
        top_loaded = [sem("top_b_loaded"), sem("top_f_loaded")]
        gathered = [sem("gathered_b"), sem("gathered_f")]
        cat_gathered, cat_copied = sem("cat_gathered"), sem("cat_copied")
        summed = [sem("summed_b"), sem("summed_f")]
        x_turned, x_hi_done, x_lo_done = ([sem(f"{n}_{part}") for part in "ab"]
                                          for n in ("x_turned", "x_hi_done", "x_lo_done"))
        tail_hi_done, tail_lo_done = sem("tail_hi_done"), sem("tail_lo_done")
        hid_done, act_done = sem("hid_done"), sem("act_done")
        h_turned, h_hi_done, h_lo_done = sem("h_turned"), sem("h_hi_done"), sem("h_lo_done")
        logit_done = [sem(f"logit_done{c}") for c in range(NCH)]
        bank_free = [sem(f"bank_free{c}") for c in range(NCH)]
        row_free = [sem("row_free0"), sem("row_free1")]
        max_done, exp_done, log_done = sem("max_done"), sem("exp_done"), sem("log_done")
        result_done = sem("result_done")
        stored = [sem("stored0"), sem("stored1")]

        parts = [(slice(0, XA), slice(0, XA)), (slice(XA, XK * P), slice(NC1, NC1 + XK * P - XA))]

        pieces = [(w1t[k * P:(k + 1) * P, :], HIDDEN, w1_hi[:, k, :], w1_lo[:, k, :]) for k in range(XK)]
        pieces += [(w2t[k * P:(k + 1) * P, :], OUT, w2_hi[:, k, 0:OUT], w2_lo[:, k, 0:OUT]) for k in range(HK)]

        block = ctx.enter_context(nc.Block())

        @block.sync
        def _(sp):
            def load_piece(n):
                src, width, _, _ = pieces[n]
                sp.dma_start(rows[:, n % 3, 0:width], src).then_inc(row_loaded[n % 3], 16)

            sp.dma_start(ix_raw[:], ix_d).then_inc(ix_loaded, 16)
            for n in range(3):
                load_piece(n)
            sp.wait_ge(tails_clear, 2)
            for at in (0, 32, LO_ROW):
                sp.dma_start(w1_tail_raw[at:at + TAIL, :], w1tail_d).then_inc(tail_w_loaded, 16)
                sp.dma_start(oneh[at:at + TAIL, :], oneh_d).then_inc(oneh_loaded, 16)
            for g, top in enumerate((hvb_top, hvf_top)):
                sp.dma_start(got[g][:, NNZ * SEM:], top[0:P, :]).then_inc(top_loaded[g], 16)
            for n in range(3, len(pieces)):
                sp.wait_ge(w_lo_done, n - 2)
                load_piece(n)
            sp.dma_start(b2_all[:, 0:OUT], b2_d.to_broadcast([P, OUT])).then_inc(b2_loaded, 16)

            def load_tops(t):
                for g, top in enumerate((hvb_top, hvf_top)):
                    sp.wait_ge(summed[g], t)
                    sp.dma_start(got[g][:, NNZ * SEM:], top[bass.ds(t * P, P), :]).then_inc(top_loaded[g], 16)

            def store(t, u):
                sp.wait_ge(result_done, t + 1)
                sp.dma_start(out[bass.ds(t * P, P), :], rows[:, u, 0:OUT]).then_inc(stored[u], 16)

            def free_row(i, u):
                sp.wait_ge(stored[u], 16 * i)
                sp.sem_inc(row_free[u], 1)

            load_tops(1)
            for t in range(2):
                load_tops(t + 2)
                store(t, t)
            with sp.Fori(1, TILES // 2 - 1) as i:
                for u in range(2):
                    free_row(i, u)
                    load_tops(2 * i + u + 2)
                    store(2 * i + u, u)
            for u in range(2):
                free_row(TILES // 2 - 1, u)
                store(TILES - 2 + u, u)
            for u in range(2):
                sp.wait_ge(stored[u], 16 * (TILES // 2))

        @block.gpsimd
        def _(pool):
            for g in range(2):
                pool.memset(got[g][:, 0:NNZ * SEM], 0.0).then_inc(zeroed[g][0], 1)
            pool.memset(identity[:], 0.0).then_inc(ident_zero, 1)
            pool.wait_ge(ident_zero, 1)
            pool.affine_select(out=identity[:], in_=identity[:], compare_op=ALU.not_equal, fill=1.0, base=0,
                               pattern=[[-1, P]], channel_multiplier=1).then_inc(ident_done, 1)

            last_hvec, last_cat = pool.to_reg(HVEC_V - 1), pool.to_reg(CAT_V - 1)

            def gather(n, u):
                pool.wait_ge(ix_loaded, 16)
                pool.wait_ge(ix_staged[u], n)
                pool.wait_ge(cat_free[u], n)
                pool.indirect_dma_start(
                    out=got_cat[:], out_offset=None, in_=cat_tab,
                    in_offset=bass.IndirectOffsetOnAxis(ap=ix_now[:, u, NIX - 1:NIX], axis=0),
                    bounds_check=last_cat, oob_is_err=False).then_inc(cat_gathered, 16)
                for g in range(2):
                    pool.wait_ge(ix_loaded, 16)
                    pool.wait_ge(zeroed[g][u], n)
                    for j in range(NNZ):
                        at = g * NNZ + j
                        pool.indirect_dma_start(
                            out=got[g][:, j * SEM:(j + 1) * SEM], out_offset=None, in_=hvec_tab,
                            in_offset=bass.IndirectOffsetOnAxis(ap=ix_now[:, u, at:at + 1], axis=0),
                            bounds_check=last_hvec, oob_is_err=False).then_inc(gathered[g], 16)

            with pool.Fori(1, TILES // 2 + 1) as n:
                for u in range(2):
                    gather(n, u)

        @block.scalar
        def _(act):
            act.preload_act_table_set("natural_log_exp_and_others")

            def zero(g, t, u):
                act.wait_ge(summed[g], t)
                act.memzero(got[g][:, 0:NNZ * SEM]).then_inc(zeroed[g][u], 1)

            def tail_hi(t, u):
                act.copy(x_tail[:, u, :], oneh[:, bass.ds(t * P, P)]).then_inc(tail_hi_done, 1)

            def x_high(part, t):
                cols, bank = parts[part]
                act.wait_ge(x_turned[part], t + 1)
                act.copy(x_hi[:, cols], turned[:, bank]).then_inc(x_hi_done[part], 1)

            def relu(t):
                act.wait_ge(hid_done, t + 1)
                act.activation(h_act[:], hid[:], ACT.Relu).then_inc(act_done, 1)

            def h_high(t, u):
                for half in range(2):
                    act.wait_ge(h_turned, 2 * t + half + 1)
                    act.copy(h_hi[:, u, half * NC1:(half + 1) * NC1],
                             turned[:, half * NC1:(half + 1) * NC1]).then_inc(h_hi_done, 1)

            def softmax_sum(t, u):
                act.wait_ge(max_done, t + 1)
                act.activation(exps[:], rows[:, u, :], ACT.Exp, bias=neg_max[:, u:u + 1],
                               accum_out=exp_sum[:, u:u + 1]).then_inc(exp_done, 1)
                act.wait_ge(exp_done, t + 1)
                act.activation(log_sum[:, u:u + 1], exp_sum[:, u:u + 1], ACT.Ln).then_inc(log_done, 1)

            def split_high(n):
                act.wait_ge(row_loaded[n % 3], 16 * (n // 3 + 1))
                act.copy(pieces[n][2], rows[:, n % 3, 0:pieces[n][1]]).then_inc(w_hi_done, 1)

            for n in range(3):
                split_high(n)
            act.wait_ge(tail_w_loaded, 48)
            act.copy(w1_tail[:], w1_tail_raw[:]).then_inc(tail_w_done, 1)
            act.wait_ge(oneh_loaded, 48)
            tail_hi(0, 0)
            for n in range(3, XK):
                split_high(n)
            x_high(0, 0)
            zero(0, 1, 1)
            for n in range(XK, XK + 4):
                split_high(n)
            x_high(1, 0)
            zero(1, 1, 1)
            for n in range(XK + 4, XK + HK):
                split_high(n)
            relu(0)
            zero(0, 2, 0)
            h_high(0, 0)

            def step(t, u, more):
                x_high(0, t + 1)
                x_high(1, t + 1)
                tail_hi(t + 1, 1 - u)
                if more:
                    zero(1, t + 2, u)
                relu(t + 1)
                if more:
                    zero(0, t + 3, 1 - u)
                h_high(t + 1, 1 - u)
                softmax_sum(t, u)

            with act.Fori(0, TILES // 2 - 1) as i:
                for u in range(2):
                    step(2 * i + u, u, True)
            step(TILES - 2, 0, False)
            softmax_sum(TILES - 1, 1)

        @block.vector
        def _(dve):
            steps = [0]

            def link(ins):
                steps[0] += 1
                ins.then_inc(ix_step, 1)
                dve.wait_ge(ix_step, steps[0])

            HV = 2 * NNZ
            dve.memset(w1_tail_raw[:], 0.0).then_inc(tails_clear, 1)
            dve.memset(oneh[:], 0.0).then_inc(tails_clear, 1)
            dve.memset(b2_all[:, OUT:], PADB).then_inc(pads_set, 1)
            dve.memset(w2_hi[:, :, OUT:].bitcast(F32), 0.0).then_inc(pads_set, 1)
            dve.memset(w2_lo[:, :, OUT:].bitcast(F32), 0.0).then_inc(pads_set, 1)
            for free in (cat_free[0], *bank_free, *row_free):
                dve.sem_inc(free, 1)

            def prepare(t0, t1):
                raw, f, neg, key = (x[:, t0:t1, :] for x in (ix_raw, ix_f, ix_neg, ix_key))
                link(dve.tensor_copy(f, raw))
                dve.tensor_scalar(neg[:, :, 0:HV], f[:, :, 0:HV], 0.0, float(HVEC_V), ALU.is_lt, ALU.mult)
                link(dve.tensor_scalar(neg[:, :, HV:], f[:, :, HV:], 0.0, float(CAT_V), ALU.is_lt, ALU.mult))
                link(dve.tensor_tensor(f, f, neg, ALU.add))
                dve.tensor_scalar(ix_all[:, t0:t1, HV:], f[:, :, HV:], 0.0, float(CAT_V - 1), ALU.max, ALU.min)
                link(dve.tensor_scalar(neg[:, :, 0:HV], f[:, :, 0:HV], 1.0, None, ALU.add))
                link(dve.scalar_tensor_tensor(out=key[:, :, 0:HV], in0=f[:, :, 0:HV], scalar=float(HVEC_V - 1),
                                              in1=neg[:, :, 0:HV], op0=ALU.is_le, op1=ALU.mult))
                for t in range(t0, t1):
                    for g in range(2):
                        last = dve.max(ix_sort[:, t, g * NNZ:(g + 1) * NNZ], ix_key[:, t, g * NNZ:(g + 1) * NNZ])
                link(last)
                sort, bad = (x[:, t0:t1, :].rearrange("p t (g j) -> p (t g) j", g=2) for x in (ix_sort, ix_bad))
                dup = ix_dup[:, t0:t1, :, :].rearrange("p t g j -> p (t g) j")
                dve.tensor_scalar(bad, sort, 0.0, MARK, ALU.is_le, ALU.mult)
                link(dve.tensor_tensor(dup[:, :, 1:], sort[:, :, 1:], sort[:, :, :NNZ - 1], ALU.is_equal))
                dve.tensor_scalar(sort, sort, 0.0, -1.0, ALU.max, ALU.add)
                link(dve.scalar_tensor_tensor(out=bad[:, :, 1:], in0=dup[:, :, 1:], scalar=MARK,
                                              in1=bad[:, :, 1:], op0=ALU.mult, op1=ALU.add))
                link(dve.tensor_tensor(ix_all[:, t0:t1, 0:HV], ix_sort[:, t0:t1, :], ix_bad[:, t0:t1, :], ALU.add))

            def stage(t, u):
                dve.tensor_copy(ix_now[:, u, :], ix_all[:, bass.ds(t, 1), :]
                                .rearrange("p a n -> p (a n)")).then_inc(ix_staged[u], 1)

            def sum_rows(g, t, u):
                dve.wait_ge(gathered[g], 16 * NNZ * (t + 1))
                dve.wait_ge(top_loaded[g], 16 * (t + 1))
                at = SYN + g * SEM
                dve.tensor_reduce(x_sum[:, u, at:at + SEM], got[g][:].rearrange("p (s d) -> p d s", s=SLOTS),
                                  AX.X, ALU.add).then_inc(summed[g], 1)

            def take_cat(t, u):
                dve.wait_ge(cat_gathered, 16 * (t + 1))
                dve.tensor_copy(x_sum[:, u, 0:SYN], got_cat[:]).then_inc(cat_copied, 1)
                dve.wait_ge(cat_copied, t + 1)
                dve.sem_inc(cat_free[1 - u], 1)

            def x_low(part, t):
                cols, bank = parts[part]
                dve.wait_ge(x_hi_done[part], t + 1)
                dve.tensor_tensor(x_lo[:, cols], turned[:, bank], x_hi[:, cols].bitcast(F32),
                                  ALU.subtract).then_inc(x_lo_done[part], 1)

            def tail_low(t, u):
                dve.wait_ge(tail_hi_done, t + 1)
                dve.tensor_tensor(x_tail[LO_ROW:TAILK, u, :], oneh[LO_ROW:TAILK, bass.ds(t * P, P)],
                                  x_tail[LO_ROW:TAILK, u, :].bitcast(F32), ALU.subtract).then_inc(tail_lo_done, 1)

            def h_low(t, u):
                for half in range(2):
                    cols = slice(half * NC1, (half + 1) * NC1)
                    dve.wait_ge(h_hi_done, 2 * t + half + 1)
                    dve.tensor_tensor(h_lo[:, u, cols], turned[:, cols], h_hi[:, u, cols].bitcast(F32),
                                      ALU.subtract).then_inc(h_lo_done, 1)

            def take_logits(c, now, u):
                dve.wait_ge(logit_done[c], now)
                cols = slice(c * CW, (c + 1) * CW)
                dve.tensor_tensor_reduce(rows[:, u, cols], logit[:, c, 0:CW], b2_all[:, cols], 1.0, -3.4e38,
                                         ALU.add, ALU.max, maxes[:, u, c:c + 1]).then_inc(bank_free[c], 1)

            def row_max(t, u):
                for c in range(NCH):
                    dve.wait_ge(bank_free[c], t + 2)
                dve.tensor_reduce(neg_max[:, u:u + 1], maxes[:, u, :], AX.X, ALU.max,
                                  negate=True).then_inc(max_done, 1)

            def result(t, u):
                dve.wait_ge(log_done, t + 1)
                dve.tensor_scalar(rows[:, u, 0:OUT], rows[:, u, 0:OUT], neg_max[:, u:u + 1], log_sum[:, u:u + 1],
                                  ALU.add, ALU.subtract).then_inc(result_done, 1)

            def split_low(n):
                dve.wait_ge(w_hi_done, n + 1)
                _, width, high, low = pieces[n]
                dve.tensor_tensor(low, rows[:, n % 3, 0:width], high.bitcast(F32), ALU.subtract)\
                   .then_inc(w_lo_done, 1)

            dve.wait_ge(ix_loaded, 16)
            prepare(0, 1)
            stage(0, 0)
            prepare(1, TILES)
            stage(1, 1)
            for n in range(3):
                split_low(n)
            dve.wait_ge(tail_w_done, 1)
            dve.tensor_tensor(w1_tail[32:32 + TAIL, :], w1_tail_raw[32:32 + TAIL, :],
                              w1_tail[32:32 + TAIL, :].bitcast(F32), ALU.subtract).then_inc(tail_w_done, 1)
            tail_low(0, 0)
            for n in range(3, XK):
                split_low(n)
            take_cat(0, 0)
            sum_rows(0, 0, 0)
            split_low(XK)
            x_low(0, 0)
            for n in range(XK + 1, XK + 4):
                split_low(n)
            sum_rows(1, 0, 0)
            x_low(1, 0)
            for n in range(XK + 4, XK + HK):
                split_low(n)
            take_cat(1, 1)
            sum_rows(0, 1, 1)
            h_low(0, 0)

            def step(t, u, i, more):
                now = t + 1
                dve.wait_ge(row_free[u], i + 1)
                dve.wait_ge(x_turned[0], now)
                if more:
                    stage(t + 2, u)
                dve.wait_ge(b2_loaded, 16)
                take_logits(0, now, u)
                x_low(0, t + 1)
                sum_rows(1, t + 1, 1 - u)
                dve.wait_ge(b2_loaded, 16)
                take_logits(1, now, u)
                x_low(1, t + 1)
                tail_low(t + 1, 1 - u)
                if more:
                    take_cat(t + 2, u)
                    sum_rows(0, t + 2, u)
                h_low(t + 1, 1 - u)
                dve.wait_ge(b2_loaded, 16)
                take_logits(2, now, u)
                row_max(t, u)
                result(t, u)

            with dve.Fori(0, TILES // 2 - 1) as i:
                for u in range(2):
                    step(2 * i + u, u, i, True)
            step(TILES - 2, 0, TILES // 2 - 1, False)
            last = TILES - 1
            dve.wait_ge(row_free[1], TILES // 2)
            for c in range(NCH):
                take_logits(c, last + 1, 1)
            row_max(last, 1)
            result(last, 1)

        @block.tensor
        def _(pe):
            def turn_x(part, t, u):
                cols, bank = parts[part]
                pe.wait_ge(summed[part], t + 1)
                if part == 0:
                    pe.wait_ge(cat_copied, t + 1)
                for k in range((cols.stop - cols.start) // P):
                    last = pe.transpose(turned[:, bank.start + k * P:bank.start + (k + 1) * P],
                                        x_sum[:, u, cols.start + k * P:cols.start + (k + 1) * P], identity[:])
                last.then_inc(x_turned[part], 1)

            def first_layer(part, t, u):
                pe.wait_ge(x_hi_done[part], t + 1)
                pe.wait_ge(x_lo_done[part], t + 1)
                if part == 0:
                    pe.wait_ge(tail_lo_done, t + 1)
                blocks = parts[part][0]
                for n in range(HIDDEN // NC1):
                    cols = slice(n * NC1, (n + 1) * NC1)
                    if part == 0:
                        pe.matmul(hid[:, cols], x_tail[:, u, :], w1_tail[:, cols], start=True, stop=False)
                    for k in range(blocks.start // P, blocks.stop // P):
                        xs = slice(k * P, (k + 1) * P)
                        pe.matmul(hid[:, cols], x_hi[:, xs], w1_hi[:, k, cols], start=False, stop=False)
                        pe.matmul(hid[:, cols], x_hi[:, xs], w1_lo[:, k, cols], start=False, stop=False)
                        last = pe.matmul(hid[:, cols], x_lo[:, xs], w1_hi[:, k, cols],
                                         start=False, stop=k == XK - 1)
                if part == 1:
                    last.then_inc(hid_done, 1)

            def turn_h(t):
                pe.wait_ge(act_done, t + 1)
                for k in range(HK):
                    ins = pe.transpose(turned[:, k * P:(k + 1) * P], h_act[:, k * P:(k + 1) * P], identity[:])
                    if k % (HK // 2) == HK // 2 - 1:
                        ins.then_inc(h_turned, 1)

            def second_layer(c, t, u, k0=0, k1=HK):
                if k0 == 0:
                    pe.wait_ge(bank_free[c], t + 1)
                cols = slice(c * CW, (c + 1) * CW)
                for k in range(k0, k1):
                    if c == 0 and k % (HK // 2) == 0:
                        pe.wait_ge(h_hi_done, 2 * t + 1 + k // (HK // 2))
                        pe.wait_ge(h_lo_done, 2 * t + 1 + k // (HK // 2))
                    ks = slice(k * P, (k + 1) * P)
                    pe.matmul(logit[:, c, 0:CW], h_hi[:, u, ks], w2_hi[:, k, cols], start=k == 0, stop=False)
                    pe.matmul(logit[:, c, 0:CW], h_hi[:, u, ks], w2_lo[:, k, cols], start=False, stop=False)
                    last = pe.matmul(logit[:, c, 0:CW], h_lo[:, u, ks], w2_hi[:, k, cols],
                                     start=False, stop=k == HK - 1)
                if k1 == HK:
                    last.then_inc(logit_done[c], 1)

            pe.wait_ge(ident_done, 1)
            turn_x(0, 0, 0)
            pe.wait_ge(w_lo_done, 3)
            pe.wait_ge(tail_w_done, 2)
            first_layer(0, 0, 0)
            turn_x(1, 0, 0)
            pe.wait_ge(w_lo_done, XK)
            first_layer(1, 0, 0)
            turn_h(0)
            pe.wait_ge(w_lo_done, XK + HK)
            pe.wait_ge(pads_set, 3)

            def step(t, u):
                second_layer(0, t, u)
                turn_x(0, t + 1, 1 - u)
                second_layer(1, t, u)
                turn_x(1, t + 1, 1 - u)
                second_layer(2, t, u, 0, 3)
                first_layer(0, t + 1, 1 - u)
                first_layer(1, t + 1, 1 - u)
                second_layer(2, t, u, 3, 5)
                turn_h(t + 1)
                second_layer(2, t, u, 5, HK)

            with pe.Fori(0, TILES // 2 - 1) as i:
                for u in range(2):
                    step(2 * i + u, u)
            step(TILES - 2, 0)
            for c in range(NCH):
                second_layer(c, TILES - 1, 1)


def kernel(r_d_onehot, r_cat_b_ix, r_hvb_ix, r_hvf_ix, r_hvb_top, r_hvf_top, L0_rec_cat_embeds,
           L0_rec_hvec_embeds, L0_rec_W1, L0_rec_b1, L0_rec_W2, L0_rec_b2):
    import numpy as np
    import concourse.bacc as bacc
    from concourse.bass_utils import run_bass_kernel_spmd as run

    ix = np.concatenate([np.asarray(r_hvb_ix), np.asarray(r_hvf_ix), np.asarray(r_cat_b_ix)[:, None]], axis=1)
    ix = ix.reshape(TILES, P, NIX).transpose(1, 0, 2)
    w1t = np.asarray(L0_rec_W1).T
    embedded = SYN + 2 * SEM
    ins = {
        "ix": ix,
        "oneh": np.concatenate([np.asarray(r_d_onehot).T, np.ones((1, BATCH), np.float32)], axis=0),
        "hvb_top": r_hvb_top,
        "hvf_top": r_hvf_top,
        "cat_tab": L0_rec_cat_embeds,
        "hvec_tab": L0_rec_hvec_embeds,
        "w1t": w1t[:embedded],
        "w1tail": np.concatenate([w1t[embedded:], np.asarray(L0_rec_b1)[None, :]], axis=0),
        "w2t": np.asarray(L0_rec_W2).T,
        "b2": np.asarray(L0_rec_b2)[None, :],
    }
    nc = bacc.Bacc("TRN2", target_bir_lowering=False, num_devices=1)
    arrays, args = {}, []
    for name, a in ins.items():
        a = np.ascontiguousarray(a)
        arrays[name + "_dram"] = a
        args.append(nc.dram_tensor(name + "_dram", a.shape, mybir.dt.from_np(a.dtype), kind="ExternalInput").ap())
    args.append(nc.dram_tensor("out_dram", (BATCH, OUT), F32, kind="ExternalOutput").ap())
    build(nc, *args)
    return run(nc, [arrays], core_ids=[0]).results[0]["out_dram"]
```

```python
import concourse.bass as bass
from concourse import mybir
from contextlib import ExitStack

F32, F32R, I32, BF16 = mybir.dt.float32, mybir.dt.float32r, mybir.dt.int32, mybir.dt.bfloat16
ALU = mybir.AluOpType
ACT = mybir.ActivationFunctionType
AX = mybir.AxisListType

P = 128
BATCH, NNZ = 1024, 8
SYN, SEM = 128, 256
CAT_V, HVEC_V = 1250, 6250
HIDDEN, OUT = 1024, 1250
NDIR = 7
TILES = BATCH // P
NIX = 2 * NNZ + 1
XK = (SYN + 2 * SEM) // P
HK = HIDDEN // P
NC1 = 512
NCH = 3
CUTS = [0, 416, 832, OUT]
W2_BLOCKS = 3
ROW = max(W2_BLOCKS * (CUTS[-1] - CUTS[-2]), OUT)
TAIL = NDIR + 1
LO_ROW = 64
TAILK = LO_ROW + TAIL
MARK = 8192.0
XA = SYN + SEM
ROWS = 4
SLOTS = NNZ + 1
ALWAYS = 3
WARM_UP = 2


def build(nc, ix_d, oneh_d, hvb_top, hvf_top, cat_tab, hvec_tab, w1t, w1tail_d, w2t, b2_d, out):
    with ExitStack() as ctx:
        def sb(name, shape, dt=F32):
            return ctx.enter_context(nc.sbuf_tensor(name, shape, dt))

        def pb(name, shape):
            return ctx.enter_context(nc.psum_tensor(name, shape, F32))

        def sem(name):
            return ctx.enter_context(nc.semaphore(name))

        w1_hi = sb("w1_hi", [P, XK, HIDDEN], F32R)
        w1_lo = sb("w1_lo", [P, XK, HIDDEN], F32R)
        w1_tail = sb("w1_tail", [TAILK, HIDDEN], F32R)
        w2_hi = sb("w2_hi", [P, HK, OUT], F32R)
        w2_lo = sb("w2_lo", [P, HK, OUT], F32R)
        b2_all = sb("b2_all", [P, OUT])
        identity = sb("identity", [P, P])
        rows = sb("rows", [P, ROWS, ROW])
        ix_raw = sb("ix_raw", [P, TILES, NIX], I32)
        h_act = sb("h_act", [P, HIDDEN])
        spots = iter(range(0, HIDDEN, TILES * NIX))

        def ix_work(width):
            at = next(spots)
            return h_act[:, at:at + TILES * width].rearrange("p (t n) -> p t n", t=TILES)

        ix_neg, ix_plus_one, ix_key = ix_work(NIX), ix_work(NIX), ix_work(NIX)
        ix_sort, ix_bad, ix_dup = ix_work(2 * NNZ), ix_work(2 * NNZ), ix_work(2 * NNZ)
        ix_valid = ix_work(2 * NNZ)
        ix_all = sb("ix_all", [P, TILES, NIX], I32)
        ix_now = sb("ix_now", [P, 2, NIX], I32)
        ones = sb("ones", [P, 1])
        col_used = sb("col_used", [1, TILES, 2, NNZ])
        gathers = sb("gathers", [1, TILES, 2], I32)
        run_sums = [sb(f"run_sum{i}", [1, TILES, 2]) for i in range(2)]
        first_by = sb("first_by", [1, 2], I32)
        gathered_by = sb("gathered_by", [1, TILES, 2], I32)
        w1_tail_raw = sb("w1_tail_raw", [P, HIDDEN])
        exps = w1_tail_raw[:].bitcast(BF16)[:, 0:OUT]
        got = [sb("got_b", [P, SLOTS * SEM]), sb("got_f", [P, SLOTS * SEM])]
        got_cat = sb("got_cat", [P, SYN])
        x_sum = sb("x_sum", [P, 2, XK * P])
        x_hi = sb("x_hi", [P, XK * P], F32R)
        x_lo = sb("x_lo", [P, XK * P], F32R)
        oneh = sb("oneh", [TAILK, BATCH])
        x_tail = sb("x_tail", [TAILK, 2, P], F32R)
        h_hi = sb("h_hi", [P, 2, HIDDEN], F32R)
        h_lo = sb("h_lo", [P, 2, HIDDEN], F32R)
        maxes = sb("maxes", [P, 2, NCH])
        neg_max = sb("neg_max", [P, 2])
        exp_sum = sb("exp_sum", [P, 2])
        log_sum = sb("log_sum", [P, 2])
        turned = pb("turned", [P, 2 * NC1])
        hid = pb("hid", [P, HIDDEN])
        logit = pb("logit", [P, NCH, NC1])

        ix_loaded, ix_step = sem("ix_loaded"), sem("ix_step")
        ones_set, valid_done, valid_counted = sem("ones_set"), sem("valid_done"), sem("valid_counted")
        gathers_known, first_known = sem("gathers_known"), sem("first_known")
        ix_staged = [sem("ix_staged0"), sem("ix_staged1")]
        cat_free = [sem("cat_free0"), sem("cat_free1")]
        oneh_loaded, tails_clear = sem("oneh_loaded"), sem("tails_clear")
        row_loaded = [sem(f"row_loaded{i}") for i in range(ROWS)]
        b2_loaded = sem("b2_loaded")
        ident_zero, ident_done = sem("ident_zero"), sem("ident_done")
        w_hi_done, w_lo_done = sem("w_hi_done"), sem("w_lo_done")
        tail_w_loaded, tail_w_done = sem("tail_w_loaded"), sem("tail_w_done")
        zeroed = [[sem(f"zeroed_{g}{u}") for u in range(2)] for g in "bf"]
        top_loaded = [sem("top_b_loaded"), sem("top_f_loaded")]
        gathered = [sem("gathered_b"), sem("gathered_f")]
        cat_gathered, cat_copied = sem("cat_gathered"), sem("cat_copied")
        summed = [sem("summed_b"), sem("summed_f")]
        x_turned, x_hi_done, x_lo_done = ([sem(f"{n}_{part}") for part in "ab"]
                                          for n in ("x_turned", "x_hi_done", "x_lo_done"))
        tail_hi_done, tail_lo_done = sem("tail_hi_done"), sem("tail_lo_done")
        hid_done, act_done = sem("hid_done"), sem("act_done")
        h_turned, h_hi_done, h_lo_done = sem("h_turned"), sem("h_hi_done"), sem("h_lo_done")
        logit_done = [sem(f"logit_done{c}") for c in range(NCH)]
        bank_free = [sem(f"bank_free{c}") for c in range(NCH)]
        row_free = [sem("row_free0"), sem("row_free1")]
        max_done, exp_done, log_done = sem("max_done"), sem("exp_done"), sem("log_done")
        result_done = sem("result_done")
        stored = [sem("stored0"), sem("stored1")]

        LAST_PARTS = (slice(0, OUT // 2), slice(OUT // 2, OUT))
        parts = [(slice(0, XA), slice(0, XA)), (slice(XA, XK * P), slice(NC1, NC1 + XK * P - XA))]

        pieces = [(w1t[k * P:(k + 1) * P, :].unsqueeze(1), w1_hi[:, k:k + 1, :], w1_lo[:, k:k + 1, :])
                  for k in range(XK)]
        for c in range(NCH):
            at, to = CUTS[c:c + 2]
            for k in range(0, HK, W2_BLOCKS):
                end = min(k + W2_BLOCKS, HK)
                pieces.append((w2t[k * P:end * P, at:to].rearrange("(k p) c -> p k c", p=P),
                               w2_hi[:, k:end, at:to], w2_lo[:, k:end, at:to]))
        CHUNK_PIECES = (len(pieces) - XK) // NCH

        def piece_row(n):
            blocks, width = pieces[n][1].shape[1:]
            return rows[:, n % ROWS, 0:blocks * width].rearrange("p (k c) -> p k c", k=blocks)

        block = ctx.enter_context(nc.Block())

        @block.sync
        def _(sp):
            def load_piece(n):
                sp.dma_start(piece_row(n), pieces[n][0]).then_inc(row_loaded[n % ROWS], 16)

            sp.dma_start(ix_raw[:], ix_d).then_inc(ix_loaded, 16)
            load_piece(0)
            for g, top in enumerate((hvb_top, hvf_top)):
                sp.dma_start(got[g][:, NNZ * SEM:], top[0:P, :]).then_inc(top_loaded[g], 16)
            for n in range(1, ROWS):
                load_piece(n)
            sp.wait_ge(tails_clear, 2)
            for at in (0, 32, LO_ROW):
                sp.dma_start(w1_tail_raw[at:at + TAIL, :], w1tail_d).then_inc(tail_w_loaded, 16)
                sp.dma_start(oneh[at:at + TAIL, :], oneh_d).then_inc(oneh_loaded, 16)
            for n in range(ROWS, len(pieces)):
                sp.wait_ge(w_lo_done, n + 1 - ROWS)
                load_piece(n)
            sp.dma_start(b2_all[:, 0:OUT], b2_d.to_broadcast([P, OUT])).then_inc(b2_loaded, 16)

            def store(t, u):
                sp.wait_ge(result_done, t + 1)
                sp.dma_start(out[bass.ds(t * P, P), :], rows[:, u, 0:OUT]).then_inc(stored[u], 16)

            def free_row(i, u):
                sp.wait_ge(stored[u], 16 * i)
                sp.sem_inc(row_free[u], 1)

            for t in range(2):
                store(t, t)
            with sp.Fori(1, TILES // 2 - 1) as i:
                for u in range(2):
                    free_row(i, u)
                    store(2 * i + u, u)
            for u in range(2):
                free_row(TILES // 2 - 1, u)
            store(TILES - 2, 0)
            for n, cols in enumerate(LAST_PARTS):
                sp.wait_ge(result_done, TILES + n)
                sp.dma_start(out[(TILES - 1) * P:, cols], rows[:, 1, cols]).then_inc(stored[1], 16)
            for u in range(2):
                sp.wait_ge(stored[u], 16 * (TILES // 2 + u))

        @block.gpsimd
        def _(pool):
            for g in range(2):
                pool.memset(got[g][:, 0:NNZ * SEM], 0.0).then_inc(zeroed[g][0], 1)
            pool.memset(identity[:], 0.0).then_inc(ident_zero, 1)
            pool.wait_ge(ident_zero, 1)
            pool.affine_select(out=identity[:], in_=identity[:], compare_op=ALU.not_equal, fill=1.0, base=0,
                               pattern=[[-1, P]], channel_multiplier=1).then_inc(ident_done, 1)

            last_hvec, last_cat = pool.to_reg(HVEC_V - 1), pool.to_reg(CAT_V - 1)

            def gather_column(g, u, j):
                at = g * NNZ + j
                pool.indirect_dma_start(
                    out=got[g][:, j * SEM:(j + 1) * SEM], out_offset=None, in_=hvec_tab,
                    in_offset=bass.IndirectOffsetOnAxis(ap=ix_now[:, u, at:at + 1], axis=0),
                    bounds_check=last_hvec, oob_is_err=False).then_inc(gathered[g], 16)

            def further_columns(g, u, columns, j):
                with pool.If(columns > j):
                    gather_column(g, u, j)
                    if j + 1 < NNZ:
                        further_columns(g, u, columns, j + 1)

            def gather(n, u):
                for g in range(2):
                    pool.wait_ge(ix_loaded, 16)
                    pool.wait_ge(ix_staged[u], n)
                    pool.wait_ge(zeroed[g][u], n)
                    for j in range(ALWAYS):
                        gather_column(g, u, j)
                    pool.wait_ge(gathers_known, 1)
                    columns = pool.value_load(gathers[0:1, bass.ds(2 * n - 2 + u, 1), g:g + 1]
                                              .rearrange("p a b -> p (a b)"), min_val=0, max_val=NNZ)
                    further_columns(g, u, columns, ALWAYS)
                    if g == 0:
                        pool.wait_ge(ix_loaded, 16)
                        pool.wait_ge(cat_free[u], n)
                        pool.indirect_dma_start(
                            out=got_cat[:], out_offset=None, in_=cat_tab,
                            in_offset=bass.IndirectOffsetOnAxis(ap=ix_now[:, u, NIX - 1:NIX], axis=0),
                            bounds_check=last_cat, oob_is_err=False).then_inc(cat_gathered, 16)

            with pool.Fori(1, TILES // 2 + 1) as n:
                for u in range(2):
                    gather(n, u)

        @block.scalar
        def _(act):
            act.preload_act_table_set("natural_log_exp_and_others")

            def refill(g, t, u):
                act.wait_ge(summed[g], t)
                act.dma_start(got[g][:, NNZ * SEM:], (hvb_top, hvf_top)[g][bass.ds(t * P, P), :])\
                   .then_inc(top_loaded[g], 16)
                act.memzero(got[g][:, 0:NNZ * SEM]).then_inc(zeroed[g][u], 1)

            def tail_hi(t, u):
                act.copy(x_tail[:, u, :], oneh[:, bass.ds(t * P, P)]).then_inc(tail_hi_done, 1)

            def x_high(part, t):
                cols, bank = parts[part]
                act.wait_ge(x_turned[part], t + 1)
                act.copy(x_hi[:, cols], turned[:, bank]).then_inc(x_hi_done[part], 1)

            def relu(t):
                act.wait_ge(hid_done, t + 1)
                act.activation(h_act[:], hid[:], ACT.Relu).then_inc(act_done, 1)

            def h_high(t, u):
                for half in range(2):
                    act.wait_ge(h_turned, 2 * t + half + 1)
                    act.copy(h_hi[:, u, half * NC1:(half + 1) * NC1],
                             turned[:, half * NC1:(half + 1) * NC1]).then_inc(h_hi_done, 1)

            def softmax_sum(t, u):
                act.wait_ge(max_done, t + 1)
                act.activation(exps, rows[:, u, 0:OUT], ACT.Exp, bias=neg_max[:, u:u + 1],
                               accum_out=exp_sum[:, u:u + 1]).then_inc(exp_done, 1)
                act.wait_ge(exp_done, t + 1)
                act.activation(log_sum[:, u:u + 1], exp_sum[:, u:u + 1], ACT.Ln).then_inc(log_done, 1)

            def split_high(n):
                act.wait_ge(row_loaded[n % ROWS], 16 * (n // ROWS + 1))
                act.copy(pieces[n][1], piece_row(n)).then_inc(w_hi_done, 1)

            for n in range(3):
                split_high(n)
            act.wait_ge(tail_w_loaded, 48)
            act.copy(w1_tail[:], w1_tail_raw[0:TAILK, :]).then_inc(tail_w_done, 1)
            act.wait_ge(oneh_loaded, 48)
            tail_hi(0, 0)
            for n in range(3, XK):
                split_high(n)
            x_high(0, 0)
            refill(0, 1, 1)
            for n in range(XK, XK + 3):
                split_high(n)
            x_high(1, 0)
            split_high(XK + 3)
            refill(1, 1, 1)
            relu(0)
            h_high(0, 0)
            for n in range(XK + 4, XK + 7):
                split_high(n)
            refill(0, 2, 0)
            tail_hi(1, 1)
            x_high(0, 1)
            for n in range(XK + 7, len(pieces)):
                split_high(n)
            x_high(1, 1)
            refill(1, 2, 0)

            def step(t, u, more):
                tail_hi(t + 1, 1 - u)
                x_high(0, t + 1)
                x_high(1, t + 1)
                if more:
                    refill(0, t + 3, 1 - u)
                relu(t + 1)
                h_high(t + 1, 1 - u)
                if more:
                    refill(1, t + 3, 1 - u)
                softmax_sum(t, u)

            relu(1)
            h_high(1, 1)
            for g in range(2):
                refill(g, 3, 1)
            softmax_sum(0, 0)
            with act.Fori(0, TILES // 2 - 2) as i:
                for u in (1, 0):
                    step(2 * i + 2 - u, u, True)
            for t in range(TILES - 3, TILES - 1):
                step(t, t % 2, False)
            softmax_sum(TILES - 1, 1)

        @block.vector
        def _(dve):
            steps = [0]

            def link(ins):
                steps[0] += 1
                ins.then_inc(ix_step, 1)
                dve.wait_ge(ix_step, steps[0])

            HV = 2 * NNZ
            dve.memset(ones[:], 1.0).then_inc(ones_set, 1)
            dve.memset(w1_tail_raw[0:TAILK, :], 0.0).then_inc(tails_clear, 1)
            dve.memset(oneh[:], 0.0).then_inc(tails_clear, 1)
            for free in (cat_free[0], *bank_free, *row_free):
                dve.sem_inc(free, 1)

            def prepare(t0, t1):
                raw, neg, plus_one, key = (x[:, t0:t1, :] for x in (ix_raw, ix_neg, ix_plus_one, ix_key))
                dve.tensor_scalar(neg[:, :, 0:HV], raw[:, :, 0:HV], 0.0, float(HVEC_V), ALU.is_lt, ALU.mult)
                link(dve.tensor_scalar(neg[:, :, HV:], raw[:, :, HV:], 0.0, float(CAT_V), ALU.is_lt, ALU.mult))
                link(dve.scalar_tensor_tensor(out=plus_one, in0=raw, scalar=1.0, in1=neg,
                                              op0=ALU.add, op1=ALU.add))
                dve.tensor_scalar(key[:, :, HV:], plus_one[:, :, HV:], 1.0, float(CAT_V), ALU.max, ALU.min)
                hv = plus_one[:, :, 0:HV]
                link(dve.scalar_tensor_tensor(out=key[:, :, 0:HV], in0=hv, scalar=float(HVEC_V), in1=hv,
                                              op0=ALU.is_le, op1=ALU.mult))
                dve.tensor_scalar(ix_all[:, t0:t1, HV:], key[:, :, HV:], -1.0, None, ALU.add)
                for t in range(t0, t1):
                    for g in range(2):
                        last = dve.max(ix_sort[:, t, g * NNZ:(g + 1) * NNZ], ix_key[:, t, g * NNZ:(g + 1) * NNZ])
                link(last)
                sort, bad, dup = (x[:, t0:t1, :].rearrange("p t (g j) -> p (t g) j", g=2)
                                  for x in (ix_sort, ix_bad, ix_dup))
                dve.tensor_scalar(ix_valid[:, t0:t1, :], ix_sort[:, t0:t1, :], 0.0, None, ALU.is_gt)\
                   .then_inc(valid_done, 1)
                dve.tensor_scalar(bad, sort, 0.0, MARK, ALU.is_le, ALU.mult)
                link(dve.tensor_tensor(dup[:, :, 1:], sort[:, :, 1:], sort[:, :, :NNZ - 1], ALU.is_equal))
                dve.tensor_scalar(sort, sort, 0.0, -1.0, ALU.max, ALU.add)
                link(dve.scalar_tensor_tensor(out=bad[:, :, 1:], in0=dup[:, :, 1:], scalar=MARK,
                                              in1=bad[:, :, 1:], op0=ALU.mult, op1=ALU.add))
                link(dve.tensor_tensor(ix_all[:, t0:t1, 0:HV], ix_sort[:, t0:t1, :], ix_bad[:, t0:t1, :], ALU.add))

            def count_gathers(t0, t1, batch):
                dve.wait_ge(valid_counted, batch)
                used, total = col_used[0:1, t0:t1, :, :], run_sums[0][0:1, t0:t1, :]
                link(dve.tensor_scalar(used.rearrange("p t g j -> p (t g j)"),
                                       logit[0:1, batch, 0:(t1 - t0) * 2 * NNZ], 0.0, None, ALU.is_gt))
                link(dve.tensor_reduce(total, used, AX.X, ALU.add))
                dve.tensor_copy(gathers[0:1, t0:t1, :], total).then_inc(gathers_known, 1)

            def sum_gathers():
                src, dst = run_sums[1], run_sums[0]
                link(dve.tensor_scalar(src[:], dst[:], float(ALWAYS), 16.0, ALU.max, ALU.mult))
                step = 1
                while step < TILES:
                    if 2 * step >= TILES:
                        dst = gathered_by
                    dve.tensor_copy(dst[0:1, 0:step, :], src[0:1, 0:step, :])
                    link(dve.tensor_tensor(dst[0:1, step:, :], src[0:1, step:, :],
                                           src[0:1, :TILES - step, :], ALU.add))
                    step, src, dst = 2 * step, dst, src

            def stage(t, u):
                dve.tensor_copy(ix_now[:, u, :], ix_all[:, bass.ds(t, 1), :]
                                .rearrange("p a n -> p (a n)")).then_inc(ix_staged[u], 1)

            def gathers_to_see(t):
                return [dve.value_load(gathered_by[0:1, bass.ds(t, 1), g:g + 1].rearrange("p a b -> p (a b)"),
                                       min_val=16 * ALWAYS, max_val=16 * NNZ * TILES) for g in range(2)]

            def sum_rows(g, t, u, made):
                dve.wait_ge(gathered[g], made)
                dve.wait_ge(top_loaded[g], 16 * (t + 1))
                at = SYN + g * SEM
                dve.tensor_reduce(x_sum[:, u, at:at + SEM], got[g][:].rearrange("p (s d) -> p d s", s=SLOTS),
                                  AX.X, ALU.add).then_inc(summed[g], 1)

            def take_cat(t, u):
                dve.wait_ge(cat_gathered, 16 * (t + 1))
                dve.tensor_copy(x_sum[:, u, 0:SYN], got_cat[:]).then_inc(cat_copied, 1)
                dve.wait_ge(cat_copied, t + 1)
                dve.sem_inc(cat_free[1 - u], 1)

            def x_low(part, t):
                cols, bank = parts[part]
                dve.wait_ge(x_hi_done[part], t + 1)
                dve.tensor_tensor(x_lo[:, cols], turned[:, bank], x_hi[:, cols].bitcast(F32),
                                  ALU.subtract).then_inc(x_lo_done[part], 1)

            def tail_low(t, u):
                dve.wait_ge(tail_hi_done, t + 1)
                dve.tensor_tensor(x_tail[LO_ROW:TAILK, u, :], oneh[LO_ROW:TAILK, bass.ds(t * P, P)],
                                  x_tail[LO_ROW:TAILK, u, :].bitcast(F32), ALU.subtract).then_inc(tail_lo_done, 1)

            def h_low(t, u):
                for half in range(2):
                    cols = slice(half * NC1, (half + 1) * NC1)
                    dve.wait_ge(h_hi_done, 2 * t + half + 1)
                    dve.tensor_tensor(h_lo[:, u, cols], turned[:, cols], h_hi[:, u, cols].bitcast(F32),
                                      ALU.subtract).then_inc(h_lo_done, 1)

            def take_logits(c, now, u):
                dve.wait_ge(logit_done[c], now)
                cols = slice(*CUTS[c:c + 2])
                dve.tensor_tensor_reduce(rows[:, u, cols], logit[:, c, 0:cols.stop - cols.start],
                                         b2_all[:, cols], 1.0, -3.4e38, ALU.add, ALU.max,
                                         maxes[:, u, c:c + 1]).then_inc(bank_free[c], 1)

            def row_max(t, u):
                for c in range(NCH):
                    dve.wait_ge(bank_free[c], t + 2)
                dve.tensor_reduce(neg_max[:, u:u + 1], maxes[:, u, :], AX.X, ALU.max,
                                  negate=True).then_inc(max_done, 1)

            def result(t, u, cols=slice(0, OUT)):
                dve.wait_ge(log_done, t + 1)
                dve.tensor_scalar(rows[:, u, cols], rows[:, u, cols], neg_max[:, u:u + 1], log_sum[:, u:u + 1],
                                  ALU.add, ALU.subtract).then_inc(result_done, 1)

            def split_low(n):
                dve.wait_ge(w_hi_done, n + 1)
                _, high, low = pieces[n]
                dve.tensor_tensor(low, piece_row(n), high.bitcast(F32), ALU.subtract)\
                   .then_inc(w_lo_done, 1)

            dve.wait_ge(ix_loaded, 16)
            prepare(0, 1)
            stage(0, 0)
            count_gathers(0, 1, 1)
            dve.tensor_scalar(first_by[:], run_sums[0][0:1, 0, :], float(ALWAYS), 16.0, ALU.max, ALU.mult)\
               .then_inc(first_known, 1)
            prepare(1, TILES)
            for n in range(3):
                split_low(n)
            dve.wait_ge(tail_w_done, 1)
            dve.tensor_tensor(w1_tail[32:32 + TAIL, :], w1_tail_raw[32:32 + TAIL, :],
                              w1_tail[32:32 + TAIL, :].bitcast(F32), ALU.subtract).then_inc(tail_w_done, 1)
            tail_low(0, 0)
            count_gathers(1, TILES, 2)
            stage(1, 1)
            sum_gathers()
            dve.wait_ge(first_known, 1)
            made_f = dve.value_load(first_by[0:1, 1:2], min_val=16 * ALWAYS, max_val=16 * NNZ)
            x_low(0, 0)
            for done in (cat_copied, cat_free[1]):
                dve.sem_inc(done, 1)
            for n in range(3, XK):
                split_low(n)
            sum_rows(1, 0, 0, made_f)
            x_low(1, 0)
            stage(2, 0)
            for n in range(XK, XK + 3):
                split_low(n)
            made = gathers_to_see(1)
            split_low(XK + 3)
            take_cat(1, 1)
            h_low(0, 0)
            sum_rows(0, 1, 1, made[0])
            for n in range(XK + 4, XK + 6):
                split_low(n)
            sum_rows(1, 1, 1, made[1])
            tail_low(1, 1)
            x_low(0, 1)
            split_low(XK + 6)
            x_low(1, 1)
            for n in range(XK + 7, len(pieces)):
                split_low(n)
            dve.wait_ge(w_lo_done, len(pieces))

            def step(t, u, i, gather=True, stage_next=True):
                now = t + 1
                tail_low(t + 1, 1 - u)
                if gather:
                    made = gathers_to_see(t + 2)
                dve.wait_ge(row_free[u], i + 1)
                dve.wait_ge(x_turned[0], now)
                x_low(0, t + 1)
                dve.wait_ge(b2_loaded, 16)
                take_logits(0, now, u)
                if gather:
                    take_cat(t + 2, u)
                    sum_rows(0, t + 2, u, made[0])
                dve.wait_ge(b2_loaded, 16)
                take_logits(1, now, u)
                x_low(1, t + 1)
                if stage_next:
                    stage(t + 3, 1 - u)
                if gather:
                    sum_rows(1, t + 2, u, made[1])
                h_low(t + 1, 1 - u)
                dve.wait_ge(b2_loaded, 16)
                take_logits(2, now, u)
                row_max(t, u)
                result(t, u)

            made = gathers_to_see(2)
            dve.wait_ge(row_free[0], 1)
            dve.wait_ge(b2_loaded, 16)
            take_logits(0, 1, 0)
            take_cat(2, 0)
            sum_rows(0, 2, 0, made[0])
            take_logits(1, 1, 0)
            stage(3, 1)
            h_low(1, 1)
            sum_rows(1, 2, 0, made[1])
            take_logits(2, 1, 0)
            row_max(0, 0)
            result(0, 0)
            with dve.Fori(0, TILES // 2 - 2) as i:
                for u in (1, 0):
                    step(2 * i + 2 - u, u, i + 1 - u)
            step(TILES - 3, 1, TILES // 2 - 2, stage_next=False)
            step(TILES - 2, 0, TILES // 2 - 1, gather=False, stage_next=False)
            last = TILES - 1
            dve.wait_ge(row_free[1], TILES // 2)
            for c in range(NCH):
                take_logits(c, last + 1, 1)
            row_max(last, 1)
            for cols in LAST_PARTS:
                result(last, 1, cols)

        @block.tensor
        def _(pe):
            def turn_x(part, t, u):
                cols, bank = parts[part]
                pe.wait_ge(summed[part], t + 1)
                if part == 0:
                    pe.wait_ge(cat_copied, t + 1)
                for k in range((cols.stop - cols.start) // P):
                    last = pe.transpose(turned[:, bank.start + k * P:bank.start + (k + 1) * P],
                                        x_sum[:, u, cols.start + k * P:cols.start + (k + 1) * P], identity[:])
                last.then_inc(x_turned[part], 1)

            def sum_and_turn_a(made):
                pe.wait_ge(gathered[0], made)
                pe.wait_ge(top_loaded[0], 16)
                for k in range(SEM // P):
                    to = turned[:, SYN + k * P:SYN + (k + 1) * P]
                    for j in range(SLOTS):
                        at = j * SEM + k * P
                        last = pe.matmul(to, got[0][:, at:at + P], identity[:], start=j == 0, stop=j == SLOTS - 1)
                last.then_inc(summed[0], 1)
                pe.wait_ge(cat_gathered, 16)
                pe.transpose(turned[:, 0:SYN], got_cat[:], identity[:]).then_inc(x_turned[0], 1)

            def first_layer(part, t, u):
                pe.wait_ge(x_hi_done[part], t + 1)
                pe.wait_ge(x_lo_done[part], t + 1)
                if part == 0:
                    pe.wait_ge(tail_lo_done, t + 1)
                blocks = parts[part][0]
                for n in range(HIDDEN // NC1):
                    cols = slice(n * NC1, (n + 1) * NC1)
                    if part == 0:
                        pe.matmul(hid[:, cols], x_tail[:, u, :], w1_tail[:, cols], start=True, stop=False)
                    for k in range(blocks.start // P, blocks.stop // P):
                        xs = slice(k * P, (k + 1) * P)
                        pe.matmul(hid[:, cols], x_hi[:, xs], w1_hi[:, k, cols], start=False, stop=False)
                        pe.matmul(hid[:, cols], x_hi[:, xs], w1_lo[:, k, cols], start=False, stop=False)
                        last = pe.matmul(hid[:, cols], x_lo[:, xs], w1_hi[:, k, cols],
                                         start=False, stop=k == XK - 1)
                if part == 1:
                    last.then_inc(hid_done, 1)

            def turn_h(t):
                pe.wait_ge(act_done, t + 1)
                for k in range(HK):
                    ins = pe.transpose(turned[:, k * P:(k + 1) * P], h_act[:, k * P:(k + 1) * P], identity[:])
                    if k % (HK // 2) == HK // 2 - 1:
                        ins.then_inc(h_turned, 1)

            def second_layer(c, t, u, k0=0, k1=HK):
                if k0 == 0:
                    pe.wait_ge(w_lo_done, XK + (c + 1) * CHUNK_PIECES)
                    pe.wait_ge(bank_free[c], t + 1)
                cols = slice(*CUTS[c:c + 2])
                to = logit[:, c, 0:cols.stop - cols.start]
                for k in range(k0, k1):
                    if c == 0 and k % (HK // 2) == 0:
                        pe.wait_ge(h_hi_done, 2 * t + 1 + k // (HK // 2))
                        pe.wait_ge(h_lo_done, 2 * t + 1 + k // (HK // 2))
                    ks = slice(k * P, (k + 1) * P)
                    pe.matmul(to, h_hi[:, u, ks], w2_hi[:, k, cols], start=k == 0, stop=False)
                    pe.matmul(to, h_hi[:, u, ks], w2_lo[:, k, cols], start=False, stop=False)
                    last = pe.matmul(to, h_lo[:, u, ks], w2_hi[:, k, cols],
                                     start=False, stop=k == HK - 1)
                if k1 == HK:
                    last.then_inc(logit_done[c], 1)

            def keep_warm(to, count):
                for _ in range(count):
                    pe.transpose(to, identity[:], identity[:])

            pe.wait_ge(ones_set, 1)
            for batch, (t0, t1) in enumerate(((0, 1), (1, TILES))):
                pe.wait_ge(valid_done, batch + 1)
                pe.matmul(logit[0:1, batch + 1, 0:(t1 - t0) * 2 * NNZ], ones[:],
                          ix_valid[:, t0:t1, :].rearrange("p t n -> p (t n)"),
                          start=True, stop=True).then_inc(valid_counted, 1)
            pe.wait_ge(ident_done, 1)
            pe.wait_ge(first_known, 1)
            made = pe.value_load(first_by[0:1, 0:1], min_val=16 * ALWAYS, max_val=16 * NNZ)
            with pe.Fori(0, WARM_UP):
                keep_warm(turned[:, 0:P], 8)
            sum_and_turn_a(made)
            pe.wait_ge(w_lo_done, 3)
            pe.wait_ge(tail_w_done, 2)
            first_layer(0, 0, 0)
            turn_x(1, 0, 0)
            pe.wait_ge(w_lo_done, XK)
            first_layer(1, 0, 0)
            keep_warm(logit[:, 0, 0:P], 10)
            turn_h(0)
            keep_warm(hid[:, 0:P], 6)

            def step(t, u, before=2):
                second_layer(0, t, u)
                turn_x(0, t + 1, 1 - u)
                second_layer(1, t, u)
                turn_x(1, t + 1, 1 - u)
                if before:
                    second_layer(2, t, u, 0, before)
                first_layer(0, t + 1, 1 - u)
                first_layer(1, t + 1, 1 - u)
                second_layer(2, t, u, before, 5)
                turn_h(t + 1)
                second_layer(2, t, u, 5, HK)

            step(0, 0, before=0)
            with pe.Fori(0, TILES // 2 - 1) as i:
                for u in (1, 0):
                    step(2 * i + 2 - u, u)
            for c in range(NCH):
                second_layer(c, TILES - 1, 1)


def kernel(r_d_onehot, r_cat_b_ix, r_hvb_ix, r_hvf_ix, r_hvb_top, r_hvf_top, L0_rec_cat_embeds,
           L0_rec_hvec_embeds, L0_rec_W1, L0_rec_b1, L0_rec_W2, L0_rec_b2):
    import numpy as np
    import concourse.bacc as bacc
    from concourse.bass_utils import run_bass_kernel_spmd as run

    ix = np.concatenate([np.asarray(r_hvb_ix), np.asarray(r_hvf_ix), np.asarray(r_cat_b_ix)[:, None]], axis=1)
    ix = ix.reshape(TILES, P, NIX).transpose(1, 0, 2)
    w1t = np.asarray(L0_rec_W1).T
    embedded = SYN + 2 * SEM
    ins = {
        "ix": ix,
        "oneh": np.concatenate([np.asarray(r_d_onehot).T, np.ones((1, BATCH), np.float32)], axis=0),
        "hvb_top": r_hvb_top,
        "hvf_top": r_hvf_top,
        "cat_tab": L0_rec_cat_embeds,
        "hvec_tab": L0_rec_hvec_embeds,
        "w1t": w1t[:embedded],
        "w1tail": np.concatenate([w1t[embedded:], np.asarray(L0_rec_b1)[None, :]], axis=0),
        "w2t": np.asarray(L0_rec_W2).T,
        "b2": np.asarray(L0_rec_b2)[None, :],
    }
    nc = bacc.Bacc("TRN2", target_bir_lowering=False, num_devices=1)
    arrays, args = {}, []
    for name, a in ins.items():
        a = np.ascontiguousarray(a)
        arrays[name + "_dram"] = a
        args.append(nc.dram_tensor(name + "_dram", a.shape, mybir.dt.from_np(a.dtype), kind="ExternalInput").ap())
    args.append(nc.dram_tensor("out_dram", (BATCH, OUT), F32, kind="ExternalOutput").ap())
    build(nc, *args)
    return run(nc, [arrays], core_ids=[0]).results[0]["out_dram"]
```
